# Optimizing a Trainium2 kernel written in Bass

```python
import numpy as np
import jax
import jax.numpy as jnp

def _softmax(x, axis=-1):
    return jax.nn.softmax(x, axis=axis)

def _gelu(x):
    return jax.nn.gelu(x, approximate=True)

def _silu(x):
    return jax.nn.silu(x)

def _sigmoid(x):
    return jax.nn.sigmoid(x)

def _layernorm(x, axis=-1, eps=1e-05):
    m = jnp.mean(x, axis=axis, keepdims=True)
    v = jnp.var(x, axis=axis, keepdims=True)
    return (x - m) / jnp.sqrt(v + eps)

def _scatter_add(tgt, idx, src, axis=0):
    return tgt.at[idx].add(src)

def _segment_sum(src, seg, n):
    return jax.ops.segment_sum(src, seg, n)
kernel_name = 'mk_adaln_d1_jaxref_r4_0b277d'

def setup_inputs(seed: int=0):
    np.random.seed(seed)
    _w = jnp.asarray

    def _L0_attn_setup():
        import jax, jax.numpy as jnp
        import numpy as np
        DIM = 256
        NUM_HEADS = 16
        HEAD_DIM = DIM // NUM_HEADS
        key = jax.random.key(seed)
        ks = jax.random.split(key, 10)
        B, T, D = (2, 512, DIM)
        s = 1.0 / np.sqrt(D)
        inp = {'x': jax.random.normal(ks[0], (B, T, D), dtype=jnp.float32), 'W_q': jax.random.normal(ks[1], (D, D), dtype=jnp.float32) * s, 'b_q': jnp.zeros((D,), dtype=jnp.float32), 'W_k': jax.random.normal(ks[2], (D, D), dtype=jnp.float32) * s, 'b_k': jnp.zeros((D,), dtype=jnp.float32), 'W_v': jax.random.normal(ks[3], (D, D), dtype=jnp.float32) * s, 'b_v': jnp.zeros((D,), dtype=jnp.float32), 'W_o': jax.random.normal(ks[4], (D, D), dtype=jnp.float32) * s, 'b_o': jnp.zeros((D,), dtype=jnp.float32), 'W_s': jax.random.normal(ks[5], (D, D), dtype=jnp.float32) * s}
        return inp
    _L0_attn_in = _L0_attn_setup()

    def _L0_ffn_setup():
        import jax, jax.numpy as jnp
        import numpy as np
        B, S, HID, DFF, E, K = (4, 512, 256, 1024, 8, 512)
        key = jax.random.key(seed)
        ks = jax.random.split(key, 4)
        sc_h = 1.0 / np.sqrt(HID)
        sc_f = 1.0 / np.sqrt(DFF)
        return {'x': jax.random.normal(ks[0], (B, S, HID), jnp.float32), 'router_w': jax.random.normal(ks[1], (HID, E), jnp.float32) * sc_h, 'router_b': jnp.zeros((E,), jnp.float32), 'w1': jax.random.normal(ks[2], (E, HID, DFF), jnp.float32) * sc_h, 'b1': jnp.zeros((E, DFF), jnp.float32), 'w2': jax.random.normal(ks[3], (E, DFF, HID), jnp.float32) * sc_f, 'b2': jnp.zeros((E, HID), jnp.float32)}
    _L0_ffn_in = _L0_ffn_setup()
    _L0_c = _w((lambda *s: np.random.randn(*s).astype(np.float32) * 0.05)(2, 256))
    _L0_wmod = _w((lambda *s: np.random.randn(*s).astype(np.float32) * 0.05)(256, 6 * 256) * 256 ** (-0.5))
    _d = {'L0_attn_x': _L0_attn_in['x'], 'L0_attn_W_q': _L0_attn_in['W_q'], 'L0_attn_b_q': _L0_attn_in['b_q'], 'L0_attn_W_k': _L0_attn_in['W_k'], 'L0_attn_b_k': _L0_attn_in['b_k'], 'L0_attn_W_v': _L0_attn_in['W_v'], 'L0_attn_b_v': _L0_attn_in['b_v'], 'L0_attn_W_o': _L0_attn_in['W_o'], 'L0_attn_b_o': _L0_attn_in['b_o'], 'L0_attn_W_s': _L0_attn_in['W_s'], 'L0_ffn_router_w': _L0_ffn_in['router_w'], 'L0_ffn_router_b': _L0_ffn_in['router_b'], 'L0_ffn_w1': _L0_ffn_in['w1'], 'L0_ffn_b1': _L0_ffn_in['b1'], 'L0_ffn_w2': _L0_ffn_in['w2'], 'L0_ffn_b2': _L0_ffn_in['b2'], 'L0_c': _L0_c, 'L0_wmod': _L0_wmod}
    _x0 = _d['L0_attn_x']
    _d['L0_attn_x'] = jax.random.normal(jax.random.fold_in(jax.random.key(seed), 1), (2, 2048, 256), dtype=_x0.dtype)
    del _x0
    return _d

def reference(L0_attn_x, L0_attn_W_q, L0_attn_b_q, L0_attn_W_k, L0_attn_b_k, L0_attn_W_v, L0_attn_b_v, L0_attn_W_o, L0_attn_b_o, L0_attn_W_s, L0_ffn_router_w, L0_ffn_router_b, L0_ffn_w1, L0_ffn_b1, L0_ffn_w2, L0_ffn_b2, L0_c, L0_wmod):

    def _L0_attn_ref(x, W_q, b_q, W_k, b_k, W_v, b_v, W_o, b_o, W_s):
        import jax, jax.numpy as jnp
        import numpy as np
        DIM = 256
        NUM_HEADS = 16
        HEAD_DIM = DIM // NUM_HEADS
        B, T, D = x.shape
        H, Hd = (NUM_HEADS, HEAD_DIM)
        q = x @ W_q + b_q
        k = x @ W_k + b_k
        v = x @ W_v + b_v
        q = q @ W_s
        q = q.reshape(B, T, H, Hd).transpose(0, 2, 1, 3)
        k = k.reshape(B, T, H, Hd).transpose(0, 2, 1, 3)
        v = v.reshape(B, T, H, Hd).transpose(0, 2, 1, 3)
        scores = jnp.einsum('bhqd,bhkd->bhqk', q, k) / jnp.sqrt(jnp.float32(Hd))
        attn = jax.nn.softmax(scores, axis=-1)
        out = jnp.einsum('bhqk,bhkd->bhqd', attn, v)
        out = out.transpose(0, 2, 1, 3).reshape(B, T, D)
        return out @ W_o + b_o

    def _L0_ffn_ref(x, router_w, router_b, w1, b1, w2, b2):
        import jax, jax.numpy as jnp
        import numpy as np
        B, S, HID, DFF, E, K = (4, 512, 256, 1024, 8, 512)
        b, s, h = x.shape
        xf = x.reshape(-1, h)
        logits = xf @ router_w + router_b
        scores = jax.nn.softmax(logits, axis=-1)
        G, idx = jax.lax.top_k(scores.T, K)
        toks = xf[idx]
        h1 = jax.nn.relu(jnp.einsum('ekh,ehf->ekf', toks, w1) + b1[:, None, :])
        eo = jnp.einsum('ekf,efh->ekh', h1, w2) + b2[:, None, :]
        contrib = (eo * G[..., None]).reshape(-1, h)
        y = jnp.zeros_like(xf).at[idx.reshape(-1)].add(contrib)
        return y.reshape(b, s, h)
    x = L0_attn_x
    mod = (_silu(L0_c) @ L0_wmod).reshape(L0_c.shape[0], 6, 1, -1)
    sa, ca, ga, sb, cb, gb = (mod[:, 0], mod[:, 1], mod[:, 2], mod[:, 3], mod[:, 4], mod[:, 5])
    ga = (2 * (ga >= 0) - 1) * jnp.maximum(jnp.abs(ga), 0.25)
    gb = (2 * (gb >= 0) - 1) * jnp.maximum(jnp.abs(gb), 0.25)
    h = _layernorm(x, axis=-1) * (1 + ca) + sa
    x = x + ga * _L0_attn_ref(h, L0_attn_W_q, L0_attn_b_q, L0_attn_W_k, L0_attn_b_k, L0_attn_W_v, L0_attn_b_v, L0_attn_W_o, L0_attn_b_o, L0_attn_W_s)
    h = _layernorm(x, axis=-1) * (1 + cb) + sb
    x = x + gb * _L0_ffn_ref(h, L0_ffn_router_w, L0_ffn_router_b, L0_ffn_w1, L0_ffn_b1, L0_ffn_w2, L0_ffn_b2)
    return x

_drawn_inputs = setup_inputs


def setup_inputs(seed=0):
    import zlib

    import numpy as np

    out = dict(_drawn_inputs(seed))
    spreads = {'L0_attn_b_q': (0.0, 0.8),
     'L0_attn_b_k': (0.0, 2.0),
     'L0_attn_b_v': (0.0, 0.275),
     'L0_attn_b_o': (0.0, 0.307),
     'L0_ffn_router_b': (0.0, 0.8),
     'L0_ffn_b1': (0.0, 0.8),
     'L0_ffn_b2': (0.0, 0.8)}
    factors = {'L0_attn_W_q': 3.173, 'L0_attn_W_k': 3.078, 'L0_attn_W_v': 2.971, 'L0_attn_W_s': 3.15}
    for name, (base, spread) in spreads.items():
        noise = np.random.default_rng([zlib.crc32(name.encode()), seed]).standard_normal(out[name].shape)
        drawn = base * np.exp(spread * noise) if base else spread * noise
        out[name] = jnp.asarray(drawn.astype(out[name].dtype))
    for name, factor in factors.items():
        out[name] = (out[name] * factor).astype(out[name].dtype)
    return out
```

```python
from contextlib import ExitStack

import concourse.bass as bass
from concourse import mybir

F32 = mybir.dt.float32
BF16 = mybir.dt.bfloat16
I32 = mybir.dt.int32
U32 = mybir.dt.uint32
ALU = mybir.AluOpType
ACT = mybir.ActivationFunctionType
AX = mybir.AxisListType

P = 128
NB = 2
T = 2048
D = 256
KD = D // P
H = 16
HD = D // H
G = NB * H
KT = T // P
NT = NB * KT
CH = 512
CT = CH // P
NCH = T // CH
EPS = 1e-5
SCALE = float(HD) ** -0.5
E = 8
FF = 1024
NF = FF // P
CAP = 512
CC = CAP // P
SPLIT = 3
PAIRS_Q = (0, 1, 2, 0, 1, 0)
PAIRS_K = (0, 0, 0, 1, 1, 2)
KROWS = HD * len(PAIRS_Q)
MROWS = KROWS + SPLIT
NBUF = 4
LEAD = 4
M_AT = 16 - LEAD + 1
O_AT = 2
LOOP_AT = O_AT + 1
ROUND = NBUF * KT
ROUNDS = G // NBUF - 1
BITS = 7
TAKEN = 2 * CAP
TOPBIT = 29


class Link:

    def __init__(self, engine, sem):
        self.engine, self.sem = engine, sem
        self.base, self.round, self.per, self.n = 0, 0, 0, 0

    def loop(self, reg, per):
        self.base += self.n
        self.round, self.per, self.n = reg, per, 0

    def end(self, rounds):
        assert self.n == self.per, (self.n, self.per)
        self.base += rounds * self.per
        self.round, self.per, self.n = 0, 0, 0

    def __call__(self, ins):
        ins.then_inc(self.sem, 1)
        self.n += 1
        self.engine.wait_ge(self.sem, self.base + self.round * self.per + self.n)


def schedule():
    before = []
    for z in range(KT + LEAD):
        before += [("max", z, c) for c in range(NCH)]
        if z == KT + 1:
            before.append(("m", 0))
    steps = []
    for s in range(G * KT):
        z, fills = s + KT + LEAD, []
        if z < G * KT:
            fills += [("max", z, c) for c in range(NCH)]
        if s % KT == M_AT and s // KT + 1 < G:
            fills.append(("m", s // KT + 1))
        if s % KT == O_AT and s >= KT:
            fills.append(("o", s // KT - 1))
        steps.append(fills)
    return before, steps


def adaln_moe_block(nc, x, w_q, b_q, w_k, b_k, w_v, b_v, w_o, b_o, w_s, router_w, router_b,
                    w1, b1, w2, b2, c, w_mod, out):
    ctx = ExitStack()
    with ctx:
        ctx.enter_context(nc.allow_non_contiguous_dma("small columns of biases"))

        def sb(name, shape, dt=F32):
            return ctx.enter_context(nc.sbuf_tensor(name, shape, dt))

        def sem(name):
            return ctx.enter_context(nc.semaphore(name))

        q_parts = nc.dram_tensor("q_parts", (SPLIT, D, NB * T), BF16, kind="Internal").ap()
        k_parts = nc.dram_tensor("k_parts", (SPLIT, D, NB * T), BF16, kind="Internal").ap()
        m_dram = nc.dram_tensor("m_rows", (SPLIT * KT, P), BF16, kind="Internal").ap()
        h2_dram = nc.dram_tensor("h2_rows", (NB * T, D), F32, kind="Internal").ap()

        ps = ctx.enter_context(nc.psum_tensor("ps", [P, 8 * 512], F32))

        def bank(i, n=1):
            return ps[:, i * 512:(i + n) * 512]

        ident = sb("ident", [P, P])
        ident_bf = sb("ident_bf", [P, P], BF16)
        iota_i = sb("iota_i", [P, P], I32)
        mod_row = sb("mod_row", [P, NB, 4, D])
        mod_col = sb("mod_col", [P, 4, KD, NB])
        gbo = sb("gbo", [P, NB, D])
        wog = sb("wog", [P, NB, KD, D])
        wo_sb = sb("wo_sb", [P, KD, D])
        bo_row = sb("bo_row", [P, D])
        rw_sb = sb("rw_sb", [P, KD, E])
        rb_row = sb("rb_row", [P, E])
        b1_col = sb("b1_col", [P, E * NF])
        b2_row = sb("b2_row", [P, E, D])
        rstd = sb("rstd", [P, NT])
        rstd2 = sb("rstd2", [P, 2, CT])
        logits = sb("logits", [P, NT, E])
        stats = sb("stats", [P, 2, CT, 6])
        mv = sb("mv", [P, NT, 2])
        nwt = sb("nwt", [P, 3, NT])
        v_all = sb("v_all", [P, NT, D])
        ao = sb("ao", [P, KT, NB * D])
        operands = sb("operands", [P, 2, NBUF, T], BF16)
        qp, kp = operands[:, 0], operands[:, 1]
        pt = sb("pt", [P, 2, T])
        v_st = sb("v_st", [P, 2, KT, 32])
        acc_sb = sb("acc_sb", [P, 512])
        rec = sb("rec", [P, CT * NCH])
        pmax = sb("pmax", [P, 2, KT * NCH])
        negm = sb("negm", [P, KT])
        msp = sb("msp", [P, P], BF16)
        m_t = sb("m_t", [SPLIT * KT, 2, P], BF16)
        stage_a = sb("stage_a", [P, 2, CT * D])
        stage_b = sb("stage_b", [P, 2, CT * D])

        x_all = ao[:, :, :].rearrange("p a b -> p (a b)").rearrange("p (t d) -> p t d", d=D)
        h_t = [pt[:, i, 0:KD * CH].rearrange("p (k t) -> p k t", k=KD) for i in range(2)]

        x_rows = x.rearrange("b (t p) d -> p (b t) d", p=P)
        out_rows = out.rearrange("b (t p) d -> p (b t) d", p=P)
        h2_rows = h2_dram.rearrange("(t p) d -> p t d", p=P)

        link_dve_sem, link_act_sem, link_pool_sem = sem("dve_step"), sem("act_step"), sem("pool_step")

        def newton(v, link, y, var, root, tmp):
            link(v.reciprocal(y, root))
            link(v.tensor_tensor(tmp, y, y, ALU.mult))
            link(v.tensor_tensor(tmp, tmp, var, ALU.mult))
            link(v.tensor_scalar(tmp, tmp, -0.5, 1.5, ALU.mult, ALU.add))
            link(v.tensor_tensor(y, y, tmp, ALU.mult))

        passed = sem("passed")
        links = {}
        chunks = NB * NCH
        pairs = chunks // 2

        with ExitStack() as s1:
            def sb1(name, shape, dt=F32):
                return s1.enter_context(nc.sbuf_tensor(name, shape, dt))

            wq_sb = sb1("wq_sb", [P, KD, D])
            ws_sb = sb1("ws_sb", [P, KD, D])
            wk_sb = sb1("wk_sb", [P, KD, D])
            wv_sb = sb1("wv_sb", [P, KD, D])
            wqt = sb1("wqt", [P, KD, D])
            wqs = sb1("wqs", [P, KD, D])
            wmod_sb = v_all[:].rearrange("p t d -> p (t d)")[:, 0:KD * 6 * D].rearrange("p (k n) -> p k n", k=KD)
            c_t = sb1("c_t", [P, 3, KD, NB])
            silu_b = sb1("silu_b", [P, KD, NB, P])
            bq_col = sb1("bq_col", [P, KD])
            bk_col = sb1("bk_col", [P, KD])
            bqs_col = sb1("bqs_col", [P, KD])
            bv_row = sb1("bv_row", [P, D])
            b1_rows = sb1("b1_rows", [E * NF, P])
            unit = sb1("unit", [P, 4, CH])
            parts = sb1("parts", [P, 4, SPLIT, CH], BF16)

            x_in = [sem(f"x_in{b}") for b in range(NB)]
            q_in = sem("q_in")
            w_in, c_in, wmod_in = sem("w_in"), sem("c_in"), sem("wmod_in")
            iota_done, ident_done = sem("iota_done"), sem("ident_done")
            exp_c, silu_done = sem("exp_c"), sem("silu_done")
            mods_full, wqt_full, wqt_out, wqs_full = (sem(n) for n in ("mods_full", "wqt_full", "wqt_out", "wqs_full"))
            x_stats, stats_done = sb1("x_stats", [P, NT, 6]), sem("stats_done")
            var_done, root_done = sem("var_done"), sem("root_done")
            b1_full = sem("b1_full")

            with nc.Block() as block:
                @block.sync
                def _(sp):
                    for b in range(NB):
                        sp.dma_start(c_t[:, 0, :, b], c[b].rearrange("(k p) -> p k", p=P),
                                     allow_slow_non_contiguous=True).then_inc(c_in, 16)
                    sp.dma_start(wmod_sb, w_mod.rearrange("(k p) n -> p k n", p=P)).then_inc(wmod_in, 16)
                    for b in range(NB):
                        sp.dma_start(x_all[:, b * KT:(b + 1) * KT, :],
                                     x[b].rearrange("(t p) d -> p t d", p=P)).then_inc(x_in[b], 16)
                    sp.dma_start(b2_row[:].rearrange("p e d -> p (e d)"),
                                 b2.rearrange("e d -> (e d)").partition_broadcast(P)).then_inc(w_in, 16)
                    sp.dma_start(rb_row[:], router_b.partition_broadcast(P)).then_inc(w_in, 16)
                    sp.dma_start(rw_sb[:], router_w.rearrange("(k p) e -> p k e", p=P)).then_inc(w_in, 16)

                @block.gpsimd
                def _(pool):
                    nc.gpsimd.iota(iota_i[:], pattern=[[1, P]], base=P, channel_multiplier=-1).then_inc(iota_done, 1)
                    nc.gpsimd.memset(v_st[:, :, :, HD:32], 0.0).then_inc(link_pool_sem, 1)
                    pool.wait_ge(link_pool_sem, 1)
                    nc.gpsimd.memset(v_st[:, :, :, HD:HD + 1], 1.0).then_inc(link_pool_sem, 1)
                    pool.wait_ge(link_pool_sem, 2)
                    nc.gpsimd.memset(msp[:], 0.0).then_inc(link_pool_sem, 1)
                    pool.wait_ge(link_pool_sem, 3)
                    nc.gpsimd.memset(kp[KROWS:P, :, :], 1.0).then_inc(link_pool_sem, 1)

                @block.scalar
                def _(act):
                    for dst, src in ((wq_sb, w_q), (ws_sb, w_s)):
                        act.dma_start(dst[:], src.rearrange("(k p) n -> p k n", p=P)).then_inc(q_in, 16)
                    for dst, src, done in ((bq_col, b_q, q_in), (bk_col, b_k, w_in)):
                        act.dma_start(dst[:], src.rearrange("(k p) -> p k", p=P),
                                      allow_slow_non_contiguous=True).then_inc(done, 16)
                    for dst, src in ((wk_sb, w_k), (wv_sb, w_v), (wo_sb, w_o)):
                        act.dma_start(dst[:], src.rearrange("(k p) n -> p k n", p=P)).then_inc(w_in, 16)
                    for dst, src in ((bv_row, b_v), (bo_row, b_o)):
                        act.dma_start(dst[:], src.partition_broadcast(P)).then_inc(w_in, 16)
                    act.dma_start(b1_rows[:], b1.rearrange("e (f p) -> (e f) p", p=P)).then_inc(w_in, 16)
                    act.wait_ge(c_in, 32)
                    nc.scalar.activation(c_t[:, 1], c_t[:, 0], ACT.Exp, scale=-1.0).then_inc(exp_c, 1)
                    act.wait_ge(mods_full, 1)
                    for b in range(NB):
                        nc.scalar.copy(mod_row[:, b].rearrange("p m d -> p (m d)"), bank(2 * b, 2))
                    act.wait_ge(var_done, 1)
                    nc.scalar.activation(nwt[:, 1], nwt[:, 0], ACT.Sqrt).then_inc(root_done, 1)

                @block.vector
                def _(dve):
                    link = links["dve"] = Link(dve, link_dve_sem)
                    v = nc.vector
                    dve.wait_ge(exp_c, 1)
                    link(v.tensor_scalar_add(c_t[:, 1], c_t[:, 1], 1.0))
                    link(v.reciprocal(c_t[:, 2], c_t[:, 1]))
                    link(v.tensor_tensor(c_t[:, 1], c_t[:, 0], c_t[:, 2], ALU.mult))
                    for k in range(KD):
                        for b in range(NB):
                            last = v.tensor_copy(silu_b[:, k, b, :], c_t[:, 1, k, b:b + 1].to_broadcast([P, P]))
                    last.then_inc(silu_done, 1)
                    dve.wait_ge(iota_done, 1)
                    v.tensor_scalar(ident[:], iota_i[:], float(P), None, ALU.is_equal).then_inc(ident_done, 1)
                    v.tensor_scalar(ident_bf[:], iota_i[:], float(P), None, ALU.is_equal).then_inc(ident_done, 1)
                    for b in range(NB):
                        dve.wait_ge(x_in[b], 16)
                        with dve.Fori(0, KT // 8) as i:
                            for t in range(8):
                                at = i * 8 + (b * KT + t)
                                last = v.bn_stats(x_stats[:, bass.ds(at, 1), :].squeeze(1), x_all[:, bass.ds(at, 1), :].squeeze(1))
                            last.then_inc(stats_done, 1)
                        if b == 0:
                            dve.wait_ge(wqt_full, 1)
                            v.tensor_copy(wqt[:].rearrange("p k d -> p (k d)"), bank(4)).then_inc(wqt_out, 1)
                    dve.wait_ge(stats_done, NT // 8)
                    half_mean, half_sum = x_stats[:, :, 1:5:3], x_stats[:, :, 2:6:3]
                    mean, var, tmp = mv[:, :, 0], nwt[:, 0], nwt[:, 2]
                    v.tensor_tensor(mean, half_mean[:, :, 0], half_mean[:, :, 1], ALU.add)
                    v.tensor_tensor(tmp, half_mean[:, :, 0], half_mean[:, :, 1], ALU.subtract)
                    link(v.tensor_tensor(var, half_sum[:, :, 0], half_sum[:, :, 1], ALU.add))
                    v.tensor_scalar(mean, mean, 0.5, None, ALU.mult)
                    v.tensor_tensor(tmp, tmp, tmp, ALU.mult)
                    link(v.tensor_scalar(var, var, 1.0 / D, EPS, ALU.mult, ALU.add))
                    v.scalar_tensor_tensor(var, tmp, 0.25, var, ALU.mult, ALU.add).then_inc(var_done, 1)
                    cols = bank(6)[:, 0:4 * KD * NB].rearrange("p (m k b) -> p m k b", m=4, k=KD)
                    v.tensor_copy(mod_col[:, 0:4:2], cols[:, 0:4:2])
                    v.tensor_scalar_add(mod_col[:, 1:4:2], cols[:, 1:4:2], 1.0)
                    dve.wait_ge(wqs_full, 1)
                    v.tensor_copy(wqs[:].rearrange("p k d -> p (k d)"), bank(5))
                    dve.wait_ge(b1_full, 1)
                    v.tensor_copy(b1_col[:], bank(7)[:, 0:E * NF])
                    v.tensor_copy(bqs_col[:], bank(7)[:, E * NF:E * NF + KD])
                    dve.wait_ge(root_done, 1)
                    newton(v, link, rstd[:], nwt[:, 0], nwt[:, 1], nwt[:, 2])

                @block.tensor
                def _(pe):
                    mm = nc.tensor.matmul
                    pe.wait_ge(wmod_in, 16)
                    pe.wait_ge(silu_done, 1)
                    for b in range(NB):
                        for half in range(2):
                            for k in range(KD):
                                mm(bank(2 * b + half), silu_b[:, k, b, :],
                                   wmod_sb[:, k, 2 * D + half * 512:2 * D + (half + 1) * 512], start=k == 0, stop=k == KD - 1)
                    for m, which in enumerate((0, 1, 3, 4)):
                        for mt in range(KD):
                            for k in range(KD):
                                at = which * D + mt * P
                                last = mm(bank(6)[:, (m * KD + mt) * NB:(m * KD + mt + 1) * NB], wmod_sb[:, k, at:at + P],
                                          c_t[:, 1, k, :], start=k == 0, stop=k == KD - 1)
                    last.then_inc(mods_full, 1)
                    pe.wait_ge(ident_done, 2)
                    pe.wait_ge(q_in, 16 * 3)
                    for i in range(KD):
                        for m in range(KD):
                            last = nc.tensor.transpose(bank(4)[:, (m * KD + i) * P:(m * KD + i + 1) * P],
                                                       wq_sb[:, i, m * P:(m + 1) * P], ident[:])
                    last.then_inc(wqt_full, 1)
                    pe.wait_ge(wqt_out, 1)
                    for i in range(KD):
                        for m in range(KD):
                            mm(bank(5)[:, i * D:(i + 1) * D], wqt[:, m, i * P:(i + 1) * P], ws_sb[:, m, :],
                               start=m == 0, stop=m == KD - 1)
                    for mt in range(KD):
                        for m in range(KD):
                            last = mm(bank(7)[:, E * NF + mt:E * NF + mt + 1], ws_sb[:, m, mt * P:(mt + 1) * P], bq_col[:, m:m + 1],
                                      start=m == 0, stop=m == KD - 1)
                    last.then_inc(wqs_full, 1)
                    pe.wait_ge(w_in, 16 * 10)
                    nc.tensor.transpose(bank(7)[:, 0:E * NF], b1_rows[:], ident[0:E * NF, 0:E * NF]).then_inc(b1_full, 1)

            xn_ready, transposed, ht_ready = sem("xn_ready"), sem("transposed"), sem("ht_ready")
            unit_full, unit_out, v_full, v_out = sem("unit_full"), sem("unit_out"), sem("v_full"), sem("v_out")
            high_done, low_done = sem("high_done"), sem("low_done")
            stored = [sem(f"stored{u}") for u in range(4)]
            chunks = NB * NCH
            pairs = chunks // 2

            with nc.Block() as block:
                @block.sync
                def _(sp):
                    for u in range(4):
                        sp.sem_inc(stored[u], 16)
                    with sp.Fori(0, pairs) as i:
                        for par in range(2):
                            n = i * 2 + par
                            for u in range(4):
                                sp.wait_ge(low_done, n * 4 + (u + 5))
                                dst, rows = (q_parts, k_parts)[u // 2], (u % 2) * P
                                sp.dma_start(dst[:, rows:rows + P, bass.ds(n * CH, CH)].rearrange("s p t -> p s t"),
                                             parts[:, u]).then_inc(stored[u], 16)
                    for u in range(4):
                        sp.wait_ge(stored[u], 16 * chunks + 16)

                @block.vector
                def _(dve):
                    link, v = links["dve"], nc.vector
                    dve.sem_inc(low_done, 4)
                    dve.sem_inc(v_out, 2)

                    def normalise(n, par):
                        dve.wait_ge(transposed, n + 1)
                        for t in range(CT):
                            at = n * CT + t
                            last = v.tensor_scalar(stage_a[:, par, t * D:(t + 1) * D], x_all[:, bass.ds(at, 1), :].squeeze(1),
                                                   mv[:, bass.ds(at, 1), 0:1].squeeze(1), rstd[:, bass.ds(at, 1)],
                                                   ALU.subtract, ALU.mult)
                        last.then_inc(xn_ready, 1)

                    def split(n):
                        for u in range(4):
                            dve.wait_ge(high_done, n * 4 + (u + 1))
                            link(v.tensor_tensor(unit[:, u], unit[:, u], parts[:, u, 0], ALU.subtract))
                            link(v.tensor_copy(parts[:, u, 1], unit[:, u]))
                            v.tensor_tensor(parts[:, u, 2], unit[:, u], parts[:, u, 1], ALU.subtract).then_inc(low_done, 1)
                            if u % 2:
                                half = u // 2
                                dve.wait_ge(v_full, n * 2 + (half + 5))
                                v.tensor_tensor(v_all[:, bass.ds(n * CT + half * 2, 2), :],
                                                bank(6 + half).rearrange("p (t d) -> p t d", d=D),
                                                bv_row[:].unsqueeze(1).broadcast_to([P, 2, D]), ALU.add).then_inc(v_out, 1)

                    normalise(0, 0)
                    normalise(1, 1)
                    with dve.Fori(0, pairs - 1) as i:
                        link.loop(i, 16)
                        for par in range(2):
                            normalise(i * 2 + (par + 2), par)
                            split(i * 2 + par)
                    link.end(pairs - 1)
                    for n in range(chunks - 2, chunks):
                        split(n)

                @block.gpsimd
                def _(pool):
                    with pool.Fori(0, pairs) as i:
                        for par in range(2):
                            n = i * 2 + par
                            for u in range(4):
                                pool.wait_ge(unit_out, n * 4 + (u + 5))
                                pool.wait_ge(stored[u], n * 16 + 16)
                                pool.sem_inc(passed, 1)
                                nc.gpsimd.tensor_copy(parts[:, u, 0], unit[:, u]).then_inc(high_done, 1)

                @block.scalar
                def _(act):
                    act.sem_inc(unit_out, 4)
                    act.sem_inc(ht_ready, 2)

                    def modulate(n, par):
                        act.wait_ge(transposed, n + 3)
                        act.wait_ge(v_full, n * 2 + 2)
                        for k in range(KD):
                            nc.scalar.activation(h_t[par][:, k, :], bank(k), ACT.Identity,
                                                 bias=mod_col[:, 0, k, bass.ds(n // NCH, 1)],
                                                 scale=mod_col[:, 1, k, bass.ds(n // NCH, 1)]).then_inc(ht_ready, 1)

                    def take_units(n):
                        for u in range(4):
                            act.wait_ge(unit_full, n * 4 + (u + 1))
                            act.wait_ge(low_done, n * 4 + (u + 1))
                            bias = (bqs_col, bk_col)[u // 2][:, u % 2:u % 2 + 1]
                            nc.scalar.activation(unit[:, u], bank(2 + u), ACT.Identity, bias=bias).then_inc(unit_out, 1)

                    modulate(0, 0)
                    with act.Fori(0, pairs - 1) as i:
                        for par in range(2):
                            modulate(i * 2 + (par + 1), 1 - par)
                            take_units(i * 2 + par)
                    modulate(chunks - 1, 1)
                    for n in range(chunks - 2, chunks):
                        take_units(n)

                @block.tensor
                def _(pe):
                    mm = nc.tensor.matmul
                    pe.sem_inc(transposed, 2)
                    pe.sem_inc(v_full, 4)

                    def transpose_chunk(n, par):
                        pe.wait_ge(xn_ready, n + 1)
                        pe.wait_ge(ht_ready, n * 2 + 2)
                        for k in range(KD):
                            for t in range(CT):
                                last = nc.tensor.transpose(bank(k)[:, t * P:(t + 1) * P],
                                                           stage_a[:, par, t * D + k * P:t * D + (k + 1) * P], ident[:])
                        last.then_inc(transposed, 1)

                    def project(n, par):
                        pe.wait_ge(ht_ready, n * 2 + 4)
                        for u in range(4):
                            pe.wait_ge(unit_out, n * 4 + (u + 1))
                            w = (wqs, wk_sb)[u // 2]
                            for k in range(KD):
                                last = mm(bank(2 + u), w[:, k, (u % 2) * P:(u % 2 + 1) * P], h_t[par][:, k, :],
                                          start=k == 0, stop=k == KD - 1)
                            last.then_inc(unit_full, 1)
                        for half in range(2):
                            pe.wait_ge(v_out, n * 2 + (half + 1))
                            for t in range(2):
                                for k in range(KD):
                                    at = (half * 2 + t) * P
                                    last = mm(bank(6 + half)[:, t * D:(t + 1) * D], h_t[par][:, k, at:at + P],
                                              wv_sb[:, k, :], start=k == 0, stop=k == KD - 1)
                            last.then_inc(v_full, 1)

                    transpose_chunk(0, 0)
                    with pe.Fori(0, pairs - 1) as i:
                        for par in range(2):
                            transpose_chunk(i * 2 + (par + 1), 1 - par)
                            project(i * 2 + par, par)
                    transpose_chunk(chunks - 1, 1)
                    for n in range(chunks - 2, chunks):
                        project(n, n % 2)

        with_x = ExitStack()
        xb = with_x.enter_context(nc.sbuf_tensor("xb", [P, NT, D], F32))
        xb_in, xb_ready = [sem(f"xb_in{b}") for b in range(NB)], sem("xb_ready")
        with nc.Block() as block:
            before, steps = schedule()
            where, count = {}, 0
            for fills in [before] + steps:
                for fill in fills:
                    where[fill] = count
                    count += 1
            fills_of_round = sum(len(f) for f in steps[LOOP_AT:LOOP_AT + ROUND])
            assert fills_of_round % 3 == 0

            operands_in = [sem(f"operands_in{u}") for u in range(NBUF)]
            maxima_in = [sem(f"maxima_in{u}") for u in range(NBUF)]
            maxima_saved = sem("maxima_saved")
            scores_full, scores_out = sem("scores_full"), sem("scores_out")
            side_full, side_out = sem("side_full"), sem("side_out")
            pv_done, acc_out, v_staged = sem("pv_done"), sem("acc_out"), sem("v_staged")
            parts_made = sem("parts_made")

            def side_number(it, s, n_before):
                return it * fills_of_round + n_before

            def fills_until(s):
                return len(before) + sum(len(f) for f in steps[:s])

            def walk(engine, step, finish):
                for s in range(LOOP_AT):
                    step(0, s)
                with engine.Fori(0, ROUNDS) as it:
                    for s in range(LOOP_AT, LOOP_AT + ROUND):
                        step(it, s)
                for s in range(LOOP_AT, ROUND):
                    step(ROUNDS, s)
                finish()

            def fills_at(it, s):
                if isinstance(it, int):
                    at = s + it * ROUND
                    first = fills_until(at)
                    return [(first + j, f) for j, f in enumerate(steps[at])]
                first = fills_until(s)
                return [(it * fills_of_round + (first + j), f) for j, f in enumerate(steps[s])]

            def bank_of(s, j):
                return bank(5 + (fills_until(s) + j) % 3)

            def head_at(it, s, ahead=0):
                return it * NBUF + (s // KT + ahead)

            @block.sync
            def _(sp):
                def load(u, rows, cols):
                    for r, (i, j) in enumerate(zip(PAIRS_Q, PAIRS_K)):
                        sp.dma_start(qp[r * HD:(r + 1) * HD, u, :], q_parts[i, rows, cols]).then_inc(operands_in[u], 16)
                        sp.dma_start(kp[r * HD:(r + 1) * HD, u, :], k_parts[j, rows, cols]).then_inc(operands_in[u], 16)

                def place_maxima(g, u, par, number):
                    sp.wait_ge(side_out, number + 4)
                    sp.dma_start(m_dram, m_t[:, par, :]).then_inc(maxima_saved, 16)
                    sp.wait_ge(maxima_saved, g * 16 + 16)
                    sp.dma_start(qp[KROWS:MROWS, u, :], m_dram.rearrange("(s q) c -> s (q c)", s=SPLIT)).then_inc(maxima_in[u], 16)

                for g in range(NBUF):
                    load(g, slice(g * HD, (g + 1) * HD), slice(0, T))
                for b in range(NB):
                    sp.dma_start(xb[:, b * KT:(b + 1) * KT, :],
                                 x[b].rearrange("(t p) d -> p t d", p=P)).then_inc(xb_in[b], 16)
                place_maxima(0, 0, 0, where["m", 0])
                fills_of_head = fills_of_round // NBUF
                for b in range(NB):
                    first = 0 if b == 0 else H // NBUF - 1
                    rounds = H // NBUF - 1 if b == 0 else H // NBUF
                    with sp.Fori(0, rounds) as i:
                        for u in range(NBUF):
                            g = i * NBUF + (first * NBUF + u)
                            place_maxima(g + 1, (u + 1) % NBUF, (u + 1) % 2, g * fills_of_head + where["m", 1])
                            sp.wait_ge(scores_full, g * (2 * KT) + 2 * KT)
                            h = i * NBUF + (u + (NBUF if b == 0 else 0))
                            load(u, bass.ds(h * HD, HD), slice(b * T, (b + 1) * T))
                for g in range(G - NBUF + 1, G):
                    place_maxima(g, g % NBUF, g % 2, where["m", g])

            @block.gpsimd
            def _(pool):
                def stage_v(b, h, par):
                    nc.gpsimd.tensor_copy(v_st[:, par, :, 0:HD],
                                          v_all[:, b * KT:(b + 1) * KT, bass.ds(h * HD, HD)]).then_inc(v_staged, 1)

                for h in range(2):
                    stage_v(0, h, h)

                g = nc.gpsimd
                link = links["pool"] = Link(pool, link_pool_sem)
                link.base = 4
                sign, size = (stage_b[:, j, 0:NB * D].rearrange("p (b d) -> p b d", b=NB) for j in range(2))
                for m in (0, 3):
                    gates = mod_row[:, :, m, :]
                    link(g.tensor_scalar(sign, gates, 0.0, 2.0, ALU.is_ge, ALU.mult))
                    link(g.tensor_scalar(sign, sign, -1.0, None, ALU.add))
                    link(g.tensor_tensor(size, gates, sign, ALU.mult))
                    link(g.tensor_scalar(size, size, 0.25, None, ALU.max))
                    link(g.tensor_tensor(gates, size, sign, ALU.mult))
                link(g.tensor_scalar(mod_row[:, :, 2, :], mod_row[:, :, 2, :], 1.0, None, ALU.add))
                for b in range(NB):
                    ga = mod_row[:, b, 0, :]
                    link(g.tensor_tensor(wog[:, b], wo_sb[:], ga.unsqueeze(1).broadcast_to([P, KD, D]), ALU.mult))
                    link(g.tensor_tensor(gbo[:, b, :], bo_row[:], ga, ALU.mult))
                for b in range(NB):
                    pool.wait_ge(xb_in[b], 16)
                    half = KT // 2
                    for t in range(b * KT, (b + 1) * KT, half):
                        g.tensor_tensor(xb[:, t:t + half, :], xb[:, t:t + half, :],
                                        gbo[:, b:b + 1, :].broadcast_to([P, half, D]), ALU.add).then_inc(xb_ready, 1)
                link.base, link.n = link.base + link.n, 0

                for b in range(NB):
                    first = 2 if b == 0 else 0
                    with pool.Fori(0, (H - first) // 2) as i:
                        for par in range(2):
                            h = i * 2 + (first + par)
                            pool.wait_ge(pv_done, h * KT + (b * H - 1) * KT + 2)
                            pool.sem_inc(passed, 1)
                            stage_v(b, h, par)

            @block.scalar
            def _(act):
                act.sem_inc(scores_out, 2)
                act.sem_inc(acc_out, 1)

                def take_output(it, s):
                    act.wait_ge(pv_done, head_at(it, s) * KT + 2)
                    nc.scalar.copy(acc_sb[:], bank(4)).then_inc(acc_out, 1)

                def step(it, s):
                    kt = s % KT
                    y = head_at(it, s) * KT + kt
                    if kt == 1 and not (isinstance(it, int) and it * ROUND + s < KT):
                        take_output(it, s)
                    act.wait_ge(pv_done, y + 1)
                    for half in range(2):
                        act.wait_ge(scores_full, y * 2 + (half + 1))
                        nc.scalar.activation(pt[:, kt % 2, half * 1024:(half + 1) * 1024], bank(2 * half, 2),
                                             ACT.Exp, scale=SCALE).then_inc(scores_out, 1)

                walk(act, step, lambda: take_output(ROUNDS, ROUND))

            @block.vector
            def _(dve):
                v = nc.vector
                dve.sem_inc(side_out, 3)

                def take(number, fill, g, src):
                    kind = fill[0]
                    dve.wait_ge(side_full, number + 1)
                    if kind == "max":
                        z, c = fill[1:]
                        h, qt = z // KT, z % KT
                        v.reduce_max(pmax[:, h % 2, qt * NCH + c:qt * NCH + c + 1], src, AX.X).then_inc(side_out, 1)
                        if qt == KT - 1 and c == NCH - 1:
                            dve.wait_ge(side_out, number + 4)
                            step0 = g * 6
                            v.tensor_reduce(negm[:], pmax[:, h % 2, :].rearrange("p (q c) -> p q c", c=NCH),
                                            AX.X, ALU.max, negate=True).then_inc(parts_made, 1)
                            for i in range(SPLIT):
                                dve.wait_ge(parts_made, step0 + (2 * i + 1))
                                cut = v.tensor_copy(msp[:, i * KT:(i + 1) * KT], negm[:])
                                cut.then_inc(parts_made, 1)
                                if i < SPLIT - 1:
                                    dve.wait_ge(parts_made, step0 + (2 * i + 2))
                                    v.tensor_tensor(negm[:], negm[:], msp[:, i * KT:(i + 1) * KT], ALU.subtract).then_inc(parts_made, 1)
                    elif kind == "m":
                        v.tensor_copy(m_t[:, fill[1] % 2, :], src.bitcast(BF16)[0:SPLIT * KT, 0:P]).then_inc(side_out, 1)
                    else:
                        o = src.rearrange("p (c j r) -> p c j r", c=NCH, j=NCH)
                        r = rec[:].rearrange("p (c j) -> p c j", c=NCH)
                        v.reciprocal(r, o[:, :, :, HD]).then_inc(out_steps, 1)
                        dve.wait_ge(out_steps, g + 1)
                        v.tensor_tensor(ao[:, :, bass.ds(g * HD, HD)].rearrange("p (j c) d -> p c j d", c=NCH),
                                        o[:, :, :, 0:HD], r.unsqueeze(3).broadcast_to([P, NCH, NCH, HD]),
                                        ALU.mult).then_inc(side_out, 1)

                out_steps = sem("out_steps")

                def step(it, s):
                    for j, (number, fill) in enumerate(fills_at(it, s)):
                        if isinstance(it, int):
                            g = fill[1] // KT if fill[0] == "max" else fill[1]
                        elif fill[0] == "max":
                            g = it * NBUF + fill[1] // KT
                        else:
                            g = it * NBUF + fill[1]
                        take(number, fill, g, bank_of(s + (it * ROUND if isinstance(it, int) else 0), j))

                for j, fill in enumerate(before):
                    take(j, fill, 0, bank(5 + j % 3))

                def finish():
                    last_number = fills_until(G * KT)
                    dve.wait_ge(side_out, last_number + 3)
                    take(last_number, ("o", G - 1), G - 1, bank(5 + last_number % 3))

                walk(dve, step, finish)

            @block.tensor
            def _(pe):
                mm = nc.tensor.matmul
                pe.sem_inc(pv_done, 2)

                def fill_side(number, fill, rounds, dst):
                    pe.wait_ge(side_out, number + 1)
                    kind = fill[0]
                    if kind == "max":
                        z, c = fill[1:]
                        h, qt = z // KT, z % KT
                        if qt == 0 and c == 0:
                            pe.wait_ge(operands_in[h % NBUF], rounds * (16 * 12) + (h // NBUF + 1) * 16 * 12)
                        mm(dst, qp[0:KROWS, h % NBUF, qt * P:(qt + 1) * P], kp[0:KROWS, h % NBUF, c * CH:(c + 1) * CH],
                           start=True, stop=True).then_inc(side_full, 1)
                    elif kind == "m":
                        pe.wait_ge(parts_made, rounds * (NBUF * 6) + (fill[1] + 1) * 6)
                        nc.tensor.transpose(dst.bitcast(BF16)[:, 0:P], msp[:], ident_bf[:]).then_inc(side_full, 1)
                    else:
                        pe.wait_ge(acc_out, rounds * NBUF + fill[1] + 2)
                        for c in range(NCH):
                            last = nc.tensor.transpose(dst[:, c * P:(c + 1) * P], acc_sb[:, c * P:(c + 1) * P], ident[:])
                        last.then_inc(side_full, 1)

                def scores(it, s, half):
                    kt, u = s % KT, (s // KT) % NBUF
                    g = head_at(it, s)
                    if kt == 0 and half == 0:
                        pe.wait_ge(maxima_in[u], it * 16 + (s // KT // NBUF + 1) * 16)
                    pe.wait_ge(scores_out, g * (2 * KT) + (2 * kt + half + 1))
                    for j in (2 * half, 2 * half + 1):
                        last = mm(bank(j), kp[0:MROWS, u, kt * P:(kt + 1) * P], qp[0:MROWS, u, j * CH:(j + 1) * CH],
                                  start=True, stop=True)
                    last.then_inc(scores_full, 1)

                def weigh(it, s):
                    kt, par = s % KT, (s // KT) % 2
                    g = head_at(it, s)
                    if kt == 0:
                        pe.wait_ge(v_staged, g + 1)
                        pe.wait_ge(acc_out, g + 1)
                    pe.wait_ge(scores_out, g * (2 * KT) + (2 * kt + 4))
                    for j in range(NCH):
                        last = mm(bank(4)[32 * j:32 * (j + 1), :], v_st[:, par, kt, :], pt[:, kt % 2, j * CH:(j + 1) * CH],
                                  start=kt == 0, stop=kt == KT - 1)
                    last.then_inc(pv_done, 1)

                def step(it, s):
                    known = isinstance(it, int)
                    fills = list(enumerate(fills_at(it, s)))
                    rounds = 0 if known else it
                    at = s + it * ROUND if known else s

                    def side(n):
                        for _ in range(n):
                            if fills:
                                j, (number, fill) = fills.pop(0)
                                fill_side(number, fill, rounds, bank_of(at, j))

                    scores(it, s, 0)
                    side(1)
                    scores(it, s, 1)
                    side(1)
                    if not (known and at == 0):
                        weigh(it, s - 1)
                    side(len(fills))

                def finish():
                    weigh(ROUNDS, ROUND - 1)
                    fill_side(last_number, ("o", G - 1), 0, bank(5 + last_number % 3))

                last_number = fills_until(G * KT)
                for j, fill in enumerate(before):
                    fill_side(j, fill, 0, bank(5 + j % 3))
                walk(pe, step, finish)

        turned_rows = operands[:].rearrange("p a u t -> p (a u t)").bitcast(F32)
        ao_t, h2_t = (turned_rows[:, i * 2 * KD * CH:(i + 1) * 2 * KD * CH].rearrange(
            "p (s k t) -> p s k t", s=2, k=KD) for i in range(2))
        ao_c = stage_a[:].rearrange("p s (t d) -> p s t d", d=D)
        xn2 = stage_b[:].rearrange("p s (t d) -> p s t d", d=D)
        h2_c = pt[:, :, 0:CT * D].rearrange("p s (t d) -> p s t d", d=D)
        w_slots = v_all[:].rearrange("p t d -> p (t d)").rearrange("p (s n) -> p s n", s=2)
        w1_sb = [w_slots[:, s, 0:KD * FF].rearrange("p (k f) -> p k f", k=KD) for s in range(2)]
        w2_sb = [w_slots[:, s, KD * FF:].rearrange("p (f d) -> p f d", f=NF) for s in range(2)]
        w1_v = w1.rearrange("e (k p) f -> e p k f", p=P)
        w2_v = w2.rearrange("e (f p) d -> e p f d", p=P)
        weights_in = [sem(f"weights_in{s}") for s in range(2)]
        out_stored = sem("out_stored")
        h2_stored = [sem(f"h2_stored{p}") for p in range(2)]
        ao_ready, h2_ready, xn2_ready, xn2_read = (sem(n) for n in ("ao_ready", "h2_ready", "xn2_ready", "xn2_read"))
        ao_turned, aot_ready, y_full, y_out = sem("ao_turned"), sem("aot_ready"), sem("y_full"), sem("y_out")
        h2_turned, h2t_ready, l_full, l_out = sem("h2_turned"), sem("h2t_ready"), sem("l_full"), sem("l_out")
        var2_done, root2_done = sem("var2_done"), sem("root2_done")
        b_of = lambda n: bass.ds(n // NCH, 1)

        with nc.Block() as block:
            @block.sync
            def _(sp):
                for par in range(2):
                    sp.sem_inc(h2_stored[par], 16)
                for e in range(2):
                    sp.dma_start(w1_sb[e], w1_v[e]).then_inc(weights_in[e], 16)
                    sp.dma_start(w2_sb[e], w2_v[e]).then_inc(weights_in[e], 16)
                with sp.Fori(0, pairs) as i:
                    for par in range(2):
                        n = i * 2 + par
                        sp.wait_ge(y_out, n * 2 + 4)
                        sp.dma_start(out_rows[:, bass.ds(n * CT, CT), :],
                                     xb[:, bass.ds(n * CT, CT), :]).then_inc(out_stored, 16)
                        sp.wait_ge(h2_ready, n + 1)
                        sp.dma_start(h2_rows[:, bass.ds(n * CT, CT), :], h2_c[:, par]).then_inc(h2_stored[par], 16)
                sp.wait_ge(out_stored, 16 * chunks)
                for par in range(2):
                    sp.wait_ge(h2_stored[par], 16 * pairs + 16)

            @block.gpsimd
            def _(pool):
                pool.sem_inc(xn2_read, 2)
                with pool.Fori(0, pairs) as i:
                    for par in range(2):
                        n = i * 2 + par
                        pool.wait_ge(xn2_ready, n + 1)
                        pool.wait_ge(h2_stored[par], i * 16 + 16)
                        nc.gpsimd.tensor_tensor(h2_c[:, par], xn2[:, par], mod_row[:, b_of(n), 2, :].broadcast_to([P, CT, D]),
                                                ALU.mult).then_inc(xn2_read, 1)
                        pool.wait_ge(xn2_read, n + 3)
                        nc.gpsimd.tensor_tensor(h2_c[:, par], h2_c[:, par], mod_row[:, b_of(n), 1, :].broadcast_to([P, CT, D]),
                                                ALU.add).then_inc(h2_ready, 1)

            @block.scalar
            def _(act):
                def copy_ao(n, par):
                    act.wait_ge(ao_turned, n + 1)
                    nc.scalar.copy(ao_c[:, par], ao[:, bass.ds((n % NCH) * CT, CT), bass.ds((n // NCH) * D, D)]
                                   ).then_inc(ao_ready, 1)

                def take_ao(n, par):
                    act.wait_ge(ao_turned, n + 3)
                    act.wait_ge(y_full, n * 2 + 2)
                    for k in range(KD):
                        nc.scalar.copy(ao_t[:, par, k, :], bank(k)).then_inc(aot_ready, 1)

                def take_h2(n, par):
                    act.wait_ge(h2_turned, n + 3)
                    act.wait_ge(l_full, n + 1)
                    for k in range(KD):
                        nc.scalar.activation(h2_t[:, par, k, :], bank(4 + k), ACT.Identity,
                                             bias=mod_col[:, 2, k, b_of(n)], scale=mod_col[:, 3, k, b_of(n)]).then_inc(h2t_ready, 1)

                def root(n, par):
                    act.wait_ge(var2_done, n + 1)
                    nc.scalar.activation(nwt[:, 1, par * CT:(par + 1) * CT], nwt[:, 0, par * CT:(par + 1) * CT],
                                         ACT.Sqrt).then_inc(root2_done, 1)

                act.sem_inc(aot_ready, 2)
                act.sem_inc(h2t_ready, 2)

                def body(n, par, ahead=2, old=True):
                    if ahead == 2:
                        copy_ao(n + 2, par)
                    if ahead:
                        take_ao(n + 1, 1 - par)
                    if old:
                        take_h2(n - 2, par)
                    root(n, par)

                copy_ao(0, 0)
                copy_ao(1, 1)
                take_ao(0, 0)
                body(0, 0, old=False)
                body(1, 1, old=False)
                with act.Fori(1, pairs - 1) as i:
                    for par in range(2):
                        body(i * 2 + par, par)
                body(chunks - 2, 0, ahead=1)
                body(chunks - 1, 1, ahead=0)
                take_h2(chunks - 2, 0)
                take_h2(chunks - 1, 1)

            @block.vector
            def _(dve):
                link, v = links["dve"], nc.vector
                dve.sem_inc(l_out, 2)
                dve.sem_inc(y_out, 2)

                def body(n, par, logits_of):
                    for half in range(2):
                        dve.wait_ge(y_full, n * 2 + (half + 5))
                        rows = xb[:, bass.ds(n * CT + half * 2, 2), :]
                        v.tensor_tensor(rows, bank(2 + half).rearrange("p (t d) -> p t d", d=D), rows,
                                        ALU.add).then_inc(y_out, 1)
                    dve.wait_ge(y_out, n * 2 + 4)
                    dve.sem_inc(passed, 1)
                    for t in range(CT):
                        last = v.bn_stats(stats[:, par, t, :], xb[:, bass.ds(n * CT + t, 1), :].squeeze(1))
                    link(last)
                    logits_of()
                    for t in range(CT):
                        last = v.bn_aggr(mv[:, par * CT + t, :], stats[:, par, t, :])
                    link(last)
                    var, root, tmp = (nwt[:, j, par * CT:(par + 1) * CT] for j in range(3))
                    v.tensor_scalar_add(var, mv[:, par * CT:(par + 1) * CT, 1], EPS).then_inc(var2_done, 1)
                    dve.wait_ge(root2_done, n + 1)
                    newton(v, link, rstd2[:, par, :], var, root, tmp)
                    dve.wait_ge(h2_turned, n + 1)
                    dve.wait_ge(xn2_read, n + 1)
                    for t in range(CT):
                        last = v.tensor_scalar(xn2[:, par, t, :], xb[:, bass.ds(n * CT + t, 1), :].squeeze(1), mv[:, par * CT + t, 0:1],
                                               rstd2[:, par, t:t + 1], ALU.subtract, ALU.mult)
                    last.then_inc(xn2_ready, 1)

                def take_logits(n, par):
                    dve.wait_ge(l_full, n + 3)
                    v.tensor_tensor(logits[:, bass.ds(n * CT, CT), :],
                                    bank(6 + par)[:, 0:CT * E].rearrange("p (t e) -> p t e", e=E),
                                    rb_row[:].unsqueeze(1).broadcast_to([P, CT, E]), ALU.add).then_inc(l_out, 1)

                dve.wait_ge(xb_ready, 2 * NB)
                body(0, 0, lambda: None)
                body(1, 1, lambda: None)
                with dve.Fori(1, pairs) as i:
                    link.loop(i - 1, 14)
                    for par in range(2):
                        n = i * 2 + par
                        body(n, par, lambda: take_logits(n - 2, par))
                link.end(pairs - 1)
                take_logits(chunks - 2, 0)
                take_logits(chunks - 1, 1)

            @block.tensor
            def _(pe):
                mm = nc.tensor.matmul
                pe.sem_inc(ao_turned, 2)
                pe.sem_inc(y_full, 4)
                pe.sem_inc(h2_turned, 2)
                pe.sem_inc(l_full, 2)

                def turn(src, b0, done):
                    for k in range(KD):
                        for t in range(CT):
                            last = nc.tensor.transpose(bank(b0 + k)[:, t * P:(t + 1) * P], src[:, t, k * P:(k + 1) * P], ident[:])
                    last.then_inc(done, 1)

                def turn_ao(n, par):
                    pe.wait_ge(ao_ready, n + 1)
                    pe.wait_ge(aot_ready, n * 2 + 2)
                    turn(ao_c[:, par], 0, ao_turned)

                def turn_h2(n, par):
                    pe.wait_ge(xn2_ready, n + 1)
                    pe.wait_ge(h2t_ready, n * 2 + 2)
                    turn(xn2[:, par], 4, h2_turned)

                def project(n, par):
                    pe.wait_ge(aot_ready, n * 2 + 4)
                    pe.wait_ge(y_out, n * 2 + 2)
                    for half in range(2):
                        for t in range(2):
                            at = (half * 2 + t) * P
                            for k in range(KD):
                                last = mm(bank(2 + half)[:, t * D:(t + 1) * D], ao_t[:, par, k, at:at + P],
                                          wog[:, b_of(n), k, :].squeeze(1), start=k == 0, stop=k == KD - 1)
                        last.then_inc(y_full, 1)

                def route(n, par):
                    pe.wait_ge(h2t_ready, n * 2 + 4)
                    pe.wait_ge(l_out, n + 1)
                    for t in range(CT):
                        for k in range(KD):
                            last = mm(bank(6 + par)[:, t * E:(t + 1) * E], h2_t[:, par, k, t * P:(t + 1) * P],
                                      rw_sb[:, k, :], start=k == 0, stop=k == KD - 1)
                    last.then_inc(l_full, 1)

                def body(n, par, old=True, more=True):
                    if more:
                        turn_ao(n + 1, 1 - par)
                    if old:
                        turn_h2(n - 2, par)
                    project(n, par)
                    if old:
                        route(n - 2, par)

                turn_ao(0, 0)
                body(0, 0, old=False)
                body(1, 1, old=False)
                with pe.Fori(1, pairs - 1) as i:
                    for par in range(2):
                        body(i * 2 + par, par)
                body(chunks - 2, 0)
                body(chunks - 1, 1, more=False)
                for n in range(chunks - 2, chunks):
                    turn_h2(n, n % 2)
                    route(n, n % 2)
        with_x.close()

        with ExitStack() as s2:
            def sb2(name, shape, dt=F32):
                return s2.enter_context(nc.sbuf_tensor(name, shape, dt))

            peak = sb2("peak", [P, NT])
            by_row = sb2("by_row", [P, 2, P])
            above = sb2("above", [P, 2 * P], BF16)
            count = sb2("count", [P, 1], BF16)
            cand = sb2("cand", [P, 1], I32)
            flip = sb2("flip", [P, 1], I32)
            with_next = sb2("with_next", [P, 1], I32)
            half_bit = sb2("half_bit", [P, 1], I32)
            bit = sb2("bit", [P, 1])
            same = sb2("same", [P, P], BF16)
            same_i = sb2("same_i", [P, P], I32)
            ones_bf = sb2("ones_bf", [P, P], BF16)
            below = sb2("below", [P, P], BF16)
            col_row = sb2("col_row", [P, P], BF16)
            masks2 = sb2("masks2", [P, 2, 2 * P], BF16)
            masks = sb2("masks", [P, 2, E, NT], BF16)
            restart = sb2("restart", [P, E, NT], BF16)
            run = sb2("run", [P, E, NT], BF16)
            ahead = sb2("ahead", [P, E, NT], BF16)
            n_gt = sb2("n_gt", [P, E], BF16)
            n_gt_f = sb2("n_gt_f", [P, E])
            need = sb2("need", [P, E])
            sel = sb2("sel", [P, E, NT], BF16)
            place_i = sb2("place_i", [P, E, NT], I32)
            lane = sb2("lane", [P, E, NT], I32)
            quarter = sb2("quarter", [P, E, NT], I32)
            score_e = sb2("score_e", [P, E, NT])
            value = sb2("value", [P, E, NT, 5], BF16)
            in_quarter = sb2("in_quarter", [P, NT, CC], BF16)
            placed = sb2("placed", [P, NT, 32], BF16)
            one_hot = sb2("one_hot", [P, 2, 8, P], BF16)
            codes = sb2("codes", [P, CC])
            row_of = sb2("row_of", [P, CC])
            weights = sb2("weights", [P, 2, CC])
            weights_2 = sb2("weights_2", [P, 2, CC])
            list_t = sb2("list_t", [P, P])
            token_f = sb2("token_f", [P, CC])
            token = sb2("token", [P, E, CC], U32)
            gate = sb2("gate", [P, E, CC])
            second = sb2("second", [P, 2, E, CC])
            exps_in, exps_done, score_done, turned_s = sem("exps_in"), sem("exps_done"), sem("score_done"), sem("turned_s")
            counted, totalled, masks_done, masks_turned = sem("counted"), sem("totalled"), sem("masks_done"), sem("masks_turned")
            prefix_in, prefix_out, consts = sem("prefix_in"), sem("prefix_out"), sem("consts")
            hot, listed, list_out, list_made = sem("hot"), sem("listed"), sem("list_out"), sem("list_made")

            with nc.Block() as block:
                @block.gpsimd
                def _(pool):
                    g = nc.gpsimd
                    g.memset(ones_bf[:], 1.0)
                    g.iota(col_row[:], pattern=[[1, P]], base=0, channel_multiplier=0, allow_small_or_imprecise_dtypes=True)
                    g.iota(value[:, :, :, 0], pattern=[[0, E], [0, NT]], base=0, channel_multiplier=1,
                           allow_small_or_imprecise_dtypes=True)
                    g.iota(value[:, :, :, 1], pattern=[[0, E], [1, NT]], base=0, channel_multiplier=0,
                           allow_small_or_imprecise_dtypes=True)
                    g.memset(restart[:], 1.0).then_inc(link_pool_sem, 1)
                    links["pool"].n += 1
                    pool.wait_ge(link_pool_sem, links["pool"].base + links["pool"].n)
                    g.memset(restart[:, :, 0:1], 0.0).then_inc(consts, 1)
                    g.iota(codes[:], pattern=[[P, CC]], base=TAKEN, channel_multiplier=0, allow_small_or_imprecise_dtypes=True)
                    g.memset(placed[:], 0.0)
                    link = links["pool"]
                    for strip in range(4):
                        link(g.iota(row_of[32 * strip:32 * (strip + 1), :], pattern=[[-5, CC]], base=0, channel_multiplier=1,
                                    allow_small_or_imprecise_dtypes=True))
                    g.tensor_scalar(weights[:, 0, :], row_of[:], 0.0, None, ALU.is_equal)
                    g.tensor_scalar(weights_2[:, 0, :], row_of[:], 1.0, float(P), ALU.is_equal, ALU.mult)
                    g.tensor_scalar(weights[:, 1, :], row_of[:], 2.0, None, ALU.is_ge)
                    link(g.tensor_scalar(weights_2[:, 1, :], row_of[:], 4.0, None, ALU.is_le))
                    g.tensor_tensor(weights[:, 0, :], weights[:, 0, :], weights_2[:, 0, :], ALU.add)
                    g.tensor_tensor(weights[:, 1, :], weights[:, 1, :], weights_2[:, 1, :], ALU.mult)
                    pool.wait_ge(score_done, 1)
                    link(g.tensor_copy(score_e[:], logits[:].rearrange("p t e -> p e t")))
                    for i in range(SPLIT):
                        link(g.tensor_copy(value[:, :, :, 2 + i], score_e[:]))
                        if i < SPLIT - 1:
                            link(g.tensor_tensor(score_e[:], score_e[:], value[:, :, :, 2 + i], ALU.subtract))

                @block.scalar
                def _(act):
                    act.wait_ge(exps_in, 1)
                    nc.scalar.activation(logits[:], logits[:], ACT.Exp).then_inc(exps_done, 1)

                @block.vector
                def _(dve):
                    link, v = links["dve"], nc.vector
                    link(v.tensor_scalar(same_i[:], iota_i[:], E - 1, None, ALU.bitwise_and))
                    v.tensor_scalar(same[:], same_i[:], 0.0, None, ALU.is_equal)
                    v.tensor_scalar(below[:], iota_i[:], float(P), None, ALU.is_gt)
                    link(v.reduce_max(peak[:], logits[:], AX.X))
                    v.tensor_tensor(logits[:], logits[:], peak[:].unsqueeze(2).broadcast_to([P, NT, E]),
                                    ALU.subtract).then_inc(exps_in, 1)
                    dve.wait_ge(exps_done, 1)
                    link(v.reduce_sum(peak[:], logits[:], AX.X))
                    link(v.reciprocal(peak[:], peak[:]))
                    v.tensor_tensor(logits[:], logits[:], peak[:].unsqueeze(2).broadcast_to([P, NT, E]),
                                    ALU.mult).then_inc(score_done, 1)
                    v.memset(cand[:], 1 << TOPBIT)
                    link(v.memset(bit[:], float(1 << TOPBIT)))
                    dve.wait_ge(turned_s, 1)
                    link(v.tensor_copy(by_row[:], bank(0)[:, 0:2 * P].rearrange("p (a b) -> p a b", a=2)))

                    def probe(rounds, last=False):
                        v.tensor_scalar(above[:], by_row[:].rearrange("p a b -> p (a b)"), cand[:].bitcast(F32), None,
                                        ALU.is_ge, ALU.add, accum_out=count[:]).then_inc(counted, 1)
                        base = cand
                        if not last:
                            link(v.tensor_scalar(half_bit[:], bit[:], 0.5, None, ALU.mult))
                            v.tensor_tensor(with_next[:], cand[:], half_bit[:], ALU.bitwise_xor)
                            base = with_next
                        dve.wait_ge(totalled, rounds + 1)
                        link(v.tensor_scalar(flip[:], bank(1)[:, 0:1], float(CAP), bit[:], ALU.is_lt, ALU.mult))
                        if not last:
                            v.tensor_scalar(bit[:], bit[:], 0.5, None, ALU.mult)
                        link(v.tensor_tensor(cand[:], base[:], flip[:], ALU.bitwise_xor))

                    with dve.Fori(0, TOPBIT // BITS) as i:
                        link.loop(i, 3 * BITS)
                        for j in range(BITS):
                            probe(i * BITS + j)
                    link.end(TOPBIT // BITS)
                    for j in range(TOPBIT // BITS * BITS, TOPBIT):
                        probe(j)
                    probe(TOPBIT, last=True)
                    for m, op in enumerate((ALU.is_gt, ALU.is_equal)):
                        last = v.tensor_scalar(masks2[:, m, :], by_row[:].rearrange("p a b -> p (a b)"),
                                               cand[:].bitcast(F32), None, op)
                    last.then_inc(masks_done, 1)

                    dve.wait_ge(masks_turned, 1)
                    for m in range(2):
                        src = bank(2).bitcast(BF16)[:, m * 2 * P:(m + 1) * 2 * P].rearrange("p (t e) -> p e t", e=E)
                        last = v.tensor_copy(masks[:, m], src)
                    link(last)
                    gt, eq = masks[:, 0], masks[:, 1]
                    flat = lambda a: a.rearrange("p e t -> p (e t)")

                    def count_ahead(mask):
                        link(v.tensor_tensor_scan(flat(run[:]), flat(restart[:]), flat(mask), 0.0, ALU.mult, ALU.add))
                        v.tensor_tensor(ahead[:], run[:], mask, ALU.subtract).then_inc(prefix_in, 1)

                    link(v.reduce_sum(n_gt_f[:], gt, AX.X))
                    link(v.tensor_copy(n_gt[:], n_gt_f[:]))
                    dve.wait_ge(consts, 1)
                    count_ahead(eq)
                    dve.wait_ge(prefix_out, 1)
                    link(v.tensor_scalar(need[:], bank(3)[:, 0:E], -1.0, float(CAP), ALU.mult, ALU.add))
                    order = lambda b: b[:, 0:E * NT].rearrange("p (e t) -> p e t", e=E)
                    link(v.tensor_tensor(sel[:], order(bank(4)), need[:].unsqueeze(2).broadcast_to([P, E, NT]), ALU.is_lt))
                    link(v.tensor_tensor(sel[:], sel[:], eq, ALU.mult))
                    link(v.tensor_tensor(sel[:], sel[:], gt, ALU.add))
                    count_ahead(sel[:])
                    dve.wait_ge(prefix_out, 2)
                    place = bank(5)[:, 0:E * NT]
                    link(v.scalar_tensor_tensor(flat(place_i[:]), flat(sel[:]), float(TAKEN), place, ALU.mult, ALU.add))
                    v.tensor_scalar(lane[:], place_i[:], P - 1, None, ALU.bitwise_and)
                    link(v.tensor_scalar(quarter[:], place_i[:], 2 * TAKEN - P, None, ALU.bitwise_and))

                @block.tensor
                def _(pe):
                    mm = nc.tensor.matmul
                    pe.wait_ge(score_done, 1)
                    for i in range(2):
                        last = nc.tensor.transpose(bank(0)[:, i * P:(i + 1) * P],
                                                   logits[:].rearrange("p t e -> p (t e)")[:, i * P:(i + 1) * P], ident[:])
                    last.then_inc(turned_s, 1)
                    with pe.Fori(0, (TOPBIT + 1) // (BITS + 1)) as i:
                        for j in range(BITS + 1):
                            pe.wait_ge(counted, i * (BITS + 1) + (j + 1))
                            mm(bank(1)[:, 0:1], same[:], count[:], start=True, stop=True).then_inc(totalled, 1)
                    for j in range((TOPBIT + 1) // (BITS + 1) * (BITS + 1), TOPBIT + 1):
                        pe.wait_ge(counted, j + 1)
                        mm(bank(1)[:, 0:1], same[:], count[:], start=True, stop=True).then_inc(totalled, 1)
                    pe.wait_ge(masks_done, 1)
                    for m in range(2):
                        for i in range(2):
                            at = (m * 2 + i) * P
                            last = nc.tensor.transpose(bank(2).bitcast(BF16)[:, at:at + P], masks2[:, m, i * P:(i + 1) * P], ident_bf[:])
                    last.then_inc(masks_turned, 1)
                    flat = lambda a: a.rearrange("p e t -> p (e t)")
                    for j, mask in enumerate((masks[:, 1], sel[:])):
                        pe.wait_ge(prefix_in, j + 1)
                        if j == 0:
                            pe.wait_ge(consts, 1)
                            mm(bank(3)[:, 0:E], ones_bf[:], n_gt[:], start=True, stop=True)
                        mm(bank(4 + j)[:, 0:E * NT], ones_bf[:], flat(ahead[:]), start=True, stop=False)
                        mm(bank(4 + j)[:, 0:E * NT], below[:], flat(mask), start=False, stop=True).then_inc(prefix_out, 1)

            gather_at = sb2("gather_at", [P, 2, CC], U32)
            scatter_at = sb2("scatter_at", [P, 2, CC], U32)
            gb_tok = sb2("gb_tok", [P, CC, D])
            contrib = sb2("contrib", [P, CC, D])
            tok_rows = ao_c
            tok_t = stage_b[:].rearrange("p s (k t) -> p s k t", k=KD)
            hid = ao[:].rearrange("p a b -> p (a b)")[:, 0:NF * CAP].rearrange("p (f t) -> p f t", f=NF)
            rows_in = [sem(f"rows_in{p}") for p in range(2)]
            gather_set, scatter_set, added = sem("gather_set"), sem("scatter_set"), sem("added")
            tok_turned, tok_out, hid_full, hid_out = sem("tok_turned"), sem("tok_out"), sem("hid_full"), sem("hid_out")
            sums_added = sem("sums_added")
            eo_full, eo_out, contrib_ready = sem("eo_full"), sem("eo_out"), sem("contrib_ready")
            out_flat = out.rearrange("b t d -> (b t) d")

            eo_banks = (4, 5, 7, 4)

            def experts(engine, body, link=None, per=0):
                with engine.Fori(0, E // 2 - 1) as i:
                    if link:
                        link.loop(i, per)
                    for par in range(2):
                        body(i * 2 + par, i, par, True)
                if link:
                    link.end(E // 2 - 1)
                for par in range(2):
                    body(E - 2 + par, E // 2 - 1, par, False)

            with nc.Block() as block:
                @block.sync
                def _(sp):
                    def body(e, i, par, more):
                        if more:
                            sp.wait_ge(eo_full, e * CC + CC)
                            sp.dma_start(w1_sb[par], w1_v[bass.ds(e + 2, 1)].squeeze(0)).then_inc(weights_in[par], 16)
                            sp.dma_start(w2_sb[par], w2_v[bass.ds(e + 2, 1)].squeeze(0)).then_inc(weights_in[par], 16)

                    experts(sp, body)

                @block.gpsimd
                def _(pool):
                    def gather(e, par):
                        pool.wait_ge(gather_set, e + 1)
                        pool.sem_inc(passed, 1)
                        for cc in range(CC):
                            nc.gpsimd.indirect_dma_start(
                                tok_rows[:, par, cc, :], None, h2_dram,
                                bass.IndirectOffsetOnAxis(ap=gather_at[:, par, cc:cc + 1], axis=0)).then_inc(rows_in[par], 16)

                    pool.sem_inc(sums_added, 1)
                    gather(0, 0)
                    gather(1, 1)

                    def body(e, i, par, more):
                        if more:
                            pool.wait_ge(tok_turned, e + 1)
                            gather(e + 2, par)
                        pool.wait_ge(scatter_set, e + 1)
                        for cc in range(CC):
                            pool.wait_ge(contrib_ready, e * CC + (cc + 1))
                            pool.sem_inc(passed, 1)
                            nc.gpsimd.indirect_dma_start(
                                out_flat, bass.IndirectOffsetOnAxis(ap=scatter_at[:, par, cc:cc + 1], axis=0),
                                contrib[:, cc, :], None, compute_op=ALU.add).then_inc(added, 16)

                        pool.wait_ge(added, e * (16 * CC) + 16 * CC)
                        pool.sem_inc(sums_added, 1)

                    experts(pool, body)

                @block.scalar
                def _(act):
                    act.sem_inc(hid_out, 2)

                    def take_list(n):
                        act.wait_ge(listed, n * 4 + 6)
                        nc.scalar.copy(list_t[:], bank(6)[:, 0:P]).then_inc(list_out, 1)

                    take_list(0)
                    take_list(1)

                    def body(e, i, par, more):
                        for f in range(NF):
                            act.wait_ge(hid_full, e * NF + (f + 1))
                            nc.scalar.activation(hid[:, f, :], bank(2 + f % 2), ACT.Relu,
                                                 bias=b1_col[:, bass.ds(e * NF + f, 1)]).then_inc(hid_out, 1)
                        if more:
                            take_list(e + 2)

                    experts(act, body)

                @block.vector
                def _(dve):
                    link, v = links["dve"], nc.vector
                    dve.sem_inc(eo_out, CC)
                    dve.sem_inc(tok_out, 2)

                    def take_tokens(e, par):
                        dve.wait_ge(tok_turned, e + 1)
                        for k in range(KD):
                            v.tensor_copy(tok_t[:, par, k, :], bank(k)).then_inc(tok_out, 1)

                    def make_one_hot(n):
                        dve.wait_ge(listed, n * 4 + 2)
                        link(v.tensor_tensor(in_quarter[:], quarter[:, bass.ds(n, 1), :].squeeze(1).unsqueeze(2).broadcast_to([P, NT, CC]),
                                             codes[:].unsqueeze(1).broadcast_to([P, NT, CC]), ALU.is_equal))
                        link(v.tensor_tensor(placed[:, :, 0:CC * 5].rearrange("p t (c v) -> p t c v", c=CC), value[:, bass.ds(n, 1), :, :].squeeze(1).unsqueeze(2).broadcast_to([P, NT, CC, 5]),
                                             in_quarter[:].unsqueeze(3).broadcast_to([P, NT, CC, 5]), ALU.mult))
                        for g8 in range(4):
                            dve.wait_ge(listed, n * 4 + (g8 + 1))
                            v.tensor_tensor(one_hot[:, g8 % 2], lane[:, bass.ds(n, 1), g8 * 8:(g8 + 1) * 8].squeeze(1).unsqueeze(2).broadcast_to([P, 8, P]),
                                            col_row[:].unsqueeze(1).broadcast_to([P, 8, P]), ALU.is_equal).then_inc(hot, 1)

                    def take_list(n, par):
                        dve.wait_ge(list_made, n + 1)
                        made = bank(6)[:, 2 * P:2 * P + 2 * CC].rearrange("p (v c) -> p v c", v=2)
                        v.tensor_copy(gate[:, bass.ds(n, 1), :].squeeze(1), made[:, 1])
                        v.tensor_scalar(second[:, 0, bass.ds(n, 1), :].squeeze(1), made[:, 0], float(T), None, ALU.is_lt)
                        v.tensor_scalar(second[:, 1, bass.ds(n, 1), :].squeeze(1), made[:, 0], float(T), None, ALU.is_ge)
                        v.tensor_copy(token[:, bass.ds(n, 1), :].squeeze(1), made[:, 0])
                        v.tensor_copy(gather_at[:, par, :], made[:, 0]).then_inc(gather_set, 1)

                    def body(e, i, par, more):
                        if more:
                            make_one_hot(e + 2)
                        dve.wait_ge(sums_added, e + 1)
                        v.tensor_copy(scatter_at[:, par, :].unsqueeze(1), token[:, bass.ds(e, 1), :]).then_inc(scatter_set, 1)
                        for cc in range(CC):
                            last = v.tensor_scalar(gb_tok[:, cc, :], mod_row[:, 0, 3, :],
                                                   second[:, 0, bass.ds(e, 1), cc], None, ALU.mult)
                        link(last)
                        for cc in range(CC):
                            last = v.scalar_tensor_tensor(gb_tok[:, cc, :], mod_row[:, 1, 3, :],
                                                          second[:, 1, bass.ds(e, 1), cc], gb_tok[:, cc, :], ALU.mult, ALU.add)
                        link(last)
                        if more or par == 0:
                            take_tokens(e + 1, 1 - par)
                        if more:
                            dve.wait_ge(rows_in[par], i * (16 * CC) + 16 * CC)
                            take_list(e + 2, par)
                        for cc in range(CC):
                            dve.wait_ge(eo_full, e * CC + (cc + 1))
                            ins = v.tensor_tensor(contrib[:, cc, :], bank(eo_banks[cc])[:, 0:D],
                                                  b2_row[:, bass.ds(e, 1), :].squeeze(1), ALU.add)
                            ins.then_inc(eo_out, 1)
                            dve.wait_ge(eo_out, e * CC + (cc + 1 + CC))
                            v.scalar_tensor_tensor(contrib[:, cc, :], contrib[:, cc, :], gate[:, bass.ds(e, 1), cc],
                                                   gb_tok[:, cc, :], ALU.mult, ALU.mult).then_inc(contrib_ready, 1)

                    make_one_hot(0)
                    take_list(0, 0)
                    make_one_hot(1)
                    take_list(1, 1)
                    take_tokens(0, 0)
                    experts(dve, body, link, 8)

                @block.tensor
                def _(pe):
                    mm = nc.tensor.matmul

                    def turn_tokens(e, i, par):
                        pe.wait_ge(rows_in[par], i * (16 * CC) + 16 * CC)
                        pe.wait_ge(tok_out, e * 2 + 2)
                        for k in range(KD):
                            for cc in range(CC):
                                last = nc.tensor.transpose(bank(k)[:, cc * P:(cc + 1) * P],
                                                           tok_rows[:, par, cc, k * P:(k + 1) * P], ident[:])
                        last.then_inc(tok_turned, 1)

                    def sum_list(n, g8):
                        pe.wait_ge(hot, n * 4 + (g8 + 1))
                        if g8 == 0 and not (isinstance(n, int) and n == 0):
                            pe.wait_ge(gather_set, n)
                        for t in range(8):
                            tile = g8 * 8 + t
                            strip = 32 * (t % 4)
                            last = mm(bank(6)[strip:strip + 32, 0:P], placed[:, tile, :], one_hot[:, g8 % 2, t, :],
                                      start=tile < 4, stop=tile >= NT - 4)
                        last.then_inc(listed, 1)

                    def make_list(n):
                        pe.wait_ge(list_out, n + 1)
                        mm(bank(6)[:, 2 * P:2 * P + 2 * CC], list_t[:], weights[:].rearrange("r v c -> r (v c)"),
                           start=True, stop=True).then_inc(list_made, 1)

                    pe.sem_inc(listed, 2)
                    for n in range(2):
                        for g8 in range(4):
                            sum_list(n, g8)
                        make_list(n)

                    def body(e, i, par, more):
                        pe.wait_ge(weights_in[par], i * 32 + 32)
                        pe.wait_ge(tok_out, e * 2 + 4)
                        for f in range(NF):
                            pe.wait_ge(hid_out, e * NF + (f + 1))
                            for k in range(KD):
                                last = mm(bank(2 + f % 2), w1_sb[par][:, k, f * P:(f + 1) * P], tok_t[:, par, k, :],
                                          start=k == 0, stop=k == KD - 1)
                            last.then_inc(hid_full, 1)
                            if more and f % 2 == 1:
                                sum_list(e + 2, f // 2)
                        if more or par == 0:
                            turn_tokens(e + 1, i + par, 1 - par)
                        if more:
                            make_list(e + 2)
                        pe.wait_ge(hid_out, e * NF + (NF + 2))
                        for cc in range(CC):
                            pe.wait_ge(eo_out, e * CC + (CC, 2, 3, CC + 1)[cc])
                            for f in range(NF):
                                last = mm(bank(eo_banks[cc])[:, 0:D], hid[:, f, cc * P:(cc + 1) * P], w2_sb[par][:, f, :],
                                          start=f == 0, stop=f == NF - 1)
                            last.then_inc(eo_full, 1)

                    turn_tokens(0, 0, 0)
                    experts(pe, body)


_INS = ["L0_attn_x", "L0_attn_W_q", "L0_attn_b_q", "L0_attn_W_k", "L0_attn_b_k", "L0_attn_W_v", "L0_attn_b_v",
        "L0_attn_W_o", "L0_attn_b_o", "L0_attn_W_s", "L0_ffn_router_w", "L0_ffn_router_b", "L0_ffn_w1", "L0_ffn_b1",
        "L0_ffn_w2", "L0_ffn_b2", "L0_c", "L0_wmod"]


def kernel(**inputs):
    import concourse.bacc as bacc
    import numpy as np
    from concourse.bass_utils import run_bass_kernel_spmd

    nc = bacc.Bacc("TRN2", target_bir_lowering=False, num_devices=1)
    arrays, args = {}, []
    for name in _INS:
        a = np.ascontiguousarray(inputs[name])
        arrays[name] = a
        args.append(nc.dram_tensor(name, a.shape, mybir.dt.from_np(a.dtype), kind="ExternalInput").ap())
    out = nc.dram_tensor("y", (NB, T, D), F32, kind="ExternalOutput").ap()
    adaln_moe_block(nc, *args, out)
    return run_bass_kernel_spmd(nc, [arrays], core_ids=[0]).results[0]["y"]
```
